# Optimizing a Trainium2 kernel written in Bass

```python
import numpy as np
import jax
import jax.numpy as jnp

def _softmax(x, axis=-1):
    return jax.nn.softmax(x, axis=axis)

def _gelu(x):
    return jax.nn.gelu(x, approximate=True)

def _silu(x):
    return jax.nn.silu(x)

def _sigmoid(x):
    return jax.nn.sigmoid(x)

def _layernorm(x, axis=-1, eps=1e-05):
    m = jnp.mean(x, axis=axis, keepdims=True)
    v = jnp.var(x, axis=axis, keepdims=True)
    return (x - m) / jnp.sqrt(v + eps)

def _scatter_add(tgt, idx, src, axis=0):
    return tgt.at[idx].add(src)

def _segment_sum(src, seg, n):
    return jax.ops.segment_sum(src, seg, n)
kernel_name = 'mk_xattn_seq_d1_seqx_r4_342eec'

def setup_inputs(seed: int=0):
    np.random.seed(seed)
    _w = jnp.asarray

    def _rec_inputs():
        import jax
        import jax.numpy as jnp
        _rk = jax.random.key(seed)
        x = 7.22e-05 + 1 * jax.random.normal(jax.random.fold_in(_rk, 1), (2, 512, 256), jnp.float32)
        _lenS = 512 - jax.random.randint(jax.random.fold_in(_rk, 7), (2,), 0, max(1, 512 // 4) + 1, jnp.int32)
        _lenS2 = 1024 - jax.random.randint(jax.random.fold_in(_rk, 8), (2,), 0, max(1, 1024 // 4) + 1, jnp.int32)
        _ctx_1024P = jax.random.normal(jax.random.fold_in(_rk, 11), (2, 16, 256), jnp.float32)
        _ctx_1024c = jax.random.dirichlet(jax.random.fold_in(_rk, 511), 0.3 * jnp.ones((16,), jnp.float32), (2, 1024))
        _ctx_1024t = jnp.einsum('bsk,bkd->bsd', _ctx_1024c, _ctx_1024P)
        _ctx_1024t = _ctx_1024t * jax.lax.rsqrt(jnp.mean(jnp.square(_ctx_1024t)) + 1e-12) * 0.953939
        ctx_1024 = 4.13588e-05 + 0.999923 * (_ctx_1024t + 0.3 * jax.random.normal(jax.random.fold_in(_rk, 611), (2, 1024, 256), jnp.float32))
        return (x, ctx_1024)
    x, ctx_1024 = _rec_inputs()

    def _L0_xattn_setup():
        import jax, jax.numpy as jnp
        import numpy as np
        N_HEAD, M_DIM, K_DIM, V_DIM = (16, 256, 64, 64)
        LN_EPS = 1e-05
        key = jax.random.key(seed)
        ks = jax.random.split(key, 10)
        B, L = (4, 512)
        q = jax.random.normal(ks[0], (B, L, M_DIM), dtype=jnp.float32)
        k = jax.random.normal(ks[1], (B, L, M_DIM), dtype=jnp.float32)
        v = jax.random.normal(ks[2], (B, L, M_DIM), dtype=jnp.float32)
        s = 1.0 / np.sqrt(M_DIM)
        W_qs = jax.random.normal(ks[3], (M_DIM, N_HEAD * K_DIM), dtype=jnp.float32) * s
        W_ks = jax.random.normal(ks[4], (M_DIM, N_HEAD * K_DIM), dtype=jnp.float32) * s
        W_vs = jax.random.normal(ks[5], (M_DIM, N_HEAD * V_DIM), dtype=jnp.float32) * s
        fc_w = jax.random.normal(ks[6], (N_HEAD * V_DIM, M_DIM), dtype=jnp.float32) * (1.0 / np.sqrt(N_HEAD * V_DIM))
        fc_b = jnp.zeros((M_DIM,), dtype=jnp.float32)
        ln_g = jnp.ones((M_DIM,), dtype=jnp.float32)
        ln_b = jnp.zeros((M_DIM,), dtype=jnp.float32)
        return {'q': q, 'k': k, 'v': v, 'W_qs': W_qs, 'W_ks': W_ks, 'W_vs': W_vs, 'fc_w': fc_w, 'fc_b': fc_b, 'ln_g': ln_g, 'ln_b': ln_b}
    _L0_xattn_all = _L0_xattn_setup()
    _L0_xattn_in = {k: v for k, v in _L0_xattn_all.items() if k in ('W_qs', 'W_ks', 'W_vs', 'fc_w', 'fc_b', 'ln_g', 'ln_b')}
    del _L0_xattn_all
    return {'x': x, 'ctx_1024': ctx_1024, 'L0_xattn_W_qs': _L0_xattn_in['W_qs'], 'L0_xattn_W_ks': _L0_xattn_in['W_ks'], 'L0_xattn_W_vs': _L0_xattn_in['W_vs'], 'L0_xattn_fc_w': _L0_xattn_in['fc_w'], 'L0_xattn_fc_b': _L0_xattn_in['fc_b'], 'L0_xattn_ln_g': _L0_xattn_in['ln_g'], 'L0_xattn_ln_b': _L0_xattn_in['ln_b']}

def reference(x, ctx_1024, L0_xattn_W_qs, L0_xattn_W_ks, L0_xattn_W_vs, L0_xattn_fc_w, L0_xattn_fc_b, L0_xattn_ln_g, L0_xattn_ln_b):
    import jax
    import jax.numpy as jnp

    def _L0_xattn_ref(q, k, v, W_qs, W_ks, W_vs, fc_w, fc_b, ln_g, ln_b):
        import jax, jax.numpy as jnp
        import numpy as np
        N_HEAD, M_DIM, K_DIM, V_DIM = (16, 256, 64, 64)
        LN_EPS = 1e-05
        B, Lq, _ = q.shape
        residual = q
        qh = (q @ W_qs).reshape(B, Lq, N_HEAD, K_DIM)
        kh = (k @ W_ks).reshape(B, k.shape[1], N_HEAD, K_DIM)
        vh = (v @ W_vs).reshape(B, v.shape[1], N_HEAD, V_DIM)
        temperature = np.power(K_DIM, 0.5).astype(np.float32)
        attn = jnp.einsum('bqhd,bkhd->bhqk', qh, kh) / temperature
        attn = jax.nn.softmax(attn, axis=-1)
        out = jnp.einsum('bhqk,bkhd->bqhd', attn, vh).reshape(B, Lq, N_HEAD * V_DIM)
        out = out @ fc_w + fc_b
        x = out + residual
        mu = jnp.mean(x, axis=-1, keepdims=True)
        var = jnp.mean(jnp.square(x - mu), axis=-1, keepdims=True)
        return (x - mu) * jax.lax.rsqrt(var + LN_EPS) * ln_g + ln_b
    x = _L0_xattn_ref(x, ctx_1024, ctx_1024, L0_xattn_W_qs, L0_xattn_W_ks, L0_xattn_W_vs, L0_xattn_fc_w, L0_xattn_fc_b, L0_xattn_ln_g, L0_xattn_ln_b)
    return x

_drawn_inputs = setup_inputs


def setup_inputs(seed=0):
    import zlib

    import numpy as np

    out = dict(_drawn_inputs(seed))
    spreads = {'L0_xattn_fc_b': (0.0, 0.1), 'L0_xattn_ln_g': (1.0, 0.2), 'L0_xattn_ln_b': (0.0, 0.1)}
    factors = {}
    for name, (base, spread) in spreads.items():
        noise = np.random.default_rng([zlib.crc32(name.encode()), seed]).standard_normal(out[name].shape)
        drawn = base * np.exp(spread * noise) if base else spread * noise
        out[name] = jnp.asarray(drawn.astype(out[name].dtype))
    for name, factor in factors.items():
        out[name] = (out[name] * factor).astype(out[name].dtype)
    return out
```

```python
import concourse.bass as bass
from concourse import mybir
from contextlib import ExitStack

F32 = mybir.dt.float32
F32R = mybir.dt.float32r
ALU = mybir.AluOpType
ACT = mybir.ActivationFunctionType
AX = mybir.AxisListType

P = 128
B, LQ, LK, D = 2, 512, 1024, 256
HEADS, DH = 16, 64
CC = D // P
PAIRS = HEADS // 2
PHASES = PAIRS * B
QT = LQ // P
KT = LK // P
KH = LK // 512
CHUNKS = 2 * KT
UNITS = 2 * QT
SCALE = float(DH) ** -0.5
EPS = 1e-5
PRODUCTS = ((0, 0), (0, 1), (1, 0))
GROUPS = (B * LQ + B * LK) // 512 * CC


class Phase:

    def __init__(self, n, odd, pair, attend=True, prepare=True, finish=True, load_pair=True):
        self.n, self.pair = n, pair
        self.batch = odd
        self.other = 1 - odd
        self.weights_split = pair + 2 if odd else pair + 1
        self.wo_split = pair + 1 if odd else pair
        self.attend, self.prepare, self.finish = attend, prepare, finish
        self.load_pair = load_pair
        self.after_two = not (isinstance(n, int) and n < 2)
        self.first = not attend and prepare
        self.last_attend = attend and not prepare


def run_phases(engine, phase):
    phase(Phase(-1, 1, -1, attend=False, finish=False))
    phase(Phase(0, 0, 0, finish=False))
    phase(Phase(1, 1, 0))
    with engine.Fori(1, PAIRS - 1) as j:
        phase(Phase(2 * j, 0, j))
        phase(Phase(2 * j + 1, 1, j))
    phase(Phase(PHASES - 2, 0, PAIRS - 1, load_pair=False))
    phase(Phase(PHASES - 1, 1, PAIRS - 1, prepare=False, load_pair=False))
    phase(Phase(PHASES, 0, PAIRS, attend=False, prepare=False))


def build(nc, x, ctx_in, W_qs, W_ks, W_vs, fc_w, fc_b, ln_g, ln_b, out):
    stack = ExitStack()
    with stack:
        def sb(name, shape, dt=F32):
            return stack.enter_context(nc.sbuf_tensor(name, shape, dt))

        def pb(name, width=512):
            return stack.enter_context(nc.psum_tensor(name, [P, width], F32))

        def sem(name):
            return stack.enter_context(nc.semaphore(name))

        xT = [sb(f"xT_{part}", [P, CC, B * LQ], F32R) for part in ("hi", "lo")]
        cT = [sb(f"cT_{part}", [P, CC, B * LK], F32R) for part in ("hi", "lo")]
        w_raw = sb("w_raw", [P, 3, CC, P])
        w = [sb(f"w_{part}", [P, 3, CC, P], F32R) for part in ("hi", "lo")]
        wo_raw = sb("wo_raw", [P, D])
        wo = [sb(f"wo_{part}", [P, D], F32R) for part in ("hi", "lo")]
        qa = [sb(f"qa{s}", [P, 2, LQ], F32R) for s in range(2)]
        qb = [sb(f"qb{s}", [P, 2, LQ], F32R) for s in range(2)]
        ka = [sb(f"ka{s}", [P, 2, LK], F32R) for s in range(2)]
        kb = [sb(f"kb{s}", [P, 2, LK], F32R) for s in range(2)]
        v = [sb(f"v{s}", [P, KT, P]) for s in range(2)]
        probs = [sb(f"probs{s}", [P, 2, KT, LQ]) for s in range(2)]
        ksum = [sb(f"ksum{s}", [P, 2, LQ]) for s in range(2)]
        vT = sb("vT", [P, LK])
        negmax = sb("negmax", [P, UNITS])
        o_norm = sb("o_norm", [P, LQ])
        o_part = [sb(f"o_{part}", [P, LQ], F32R) for part in ("hi", "lo")]
        y = sb("y", [P, B * QT, D])
        ident = sb("ident", [P, P])
        ones = sb("ones", [P, DH])
        stats = sb("stats", [P, B * QT, 6])
        meanvar = sb("meanvar", [P, B * QT, 2])
        std = sb("std", [P, B * QT])
        rstd = sb("rstd", [P, B * QT])
        eps = sb("eps", [P, 1])
        ctx_raw = probs[1][:, :, :, :].rearrange("p e k q -> p (e k q)")[:, 0:B * KT * D] \
            .rearrange("p (t d) -> p t d", d=D)
        fcb_row = probs[0][:, 0, 0, 0:D]
        g_row = w_raw[:, 0, :, :].rearrange("p c n -> p (c n)")
        b_row = w_raw[:, 1, :, :].rearrange("p c n -> p (c n)")

        st = [pb("st0"), pb("st1")]
        sweep = pb("sweep", LK)
        aux = [pb("aux0"), pb("aux1")]
        row = pb("row")
        heads = pb("heads")
        turn = [st[0][:, :], st[1][:, :], sweep[:, 0:512], sweep[:, 512:1024]]

        x_in = [sem(f"x_in{b}") for b in range(B)]
        ctx_loaded = [sem(f"ctx_loaded{k}") for k in range(B * KH)]
        fcb_in, w_in, wo_in, gb_in, stored = (
            sem(s) for s in ("fcb_in", "w_in", "wo_in", "gb_in", "stored"))
        consts = sem("consts")
        kb_ones = sem("kb_ones")
        consts_zero = sem("consts_zero")
        y_init = sem("y_init")
        turned = sem("turned")
        turned_hi, turned_lo = sem("turned_hi"), sem("turned_lo")
        wqk_hi, wqk_split = sem("wqk_hi"), sem("wqk_split")
        wv_hi, wv_split = sem("wv_hi"), sem("wv_split")
        wo_hi, wo_split = sem("wo_hi"), sem("wo_split")
        qk_done = sem("qk_done")
        vT_done = sem("vT_done")
        vback_done = sem("vback_done")
        qk_hi = sem("qk_hi")
        qk_lo = sem("qk_lo")
        vT_kept = sem("vT_kept")
        v_kept = sem("v_kept")
        sweep_done = sem("sweep_done")
        max_done = sem("max_done")
        row_done = sem("row_done")
        row_kept = sem("row_kept")
        st_done = sem("st_done")
        exp_done = sem("exp_done")
        ksum_done = sem("ksum_done")
        denom_done = sem("denom_done")
        recip_done = sem("recip_done")
        heads_done = sem("heads_done")
        norm_done = sem("norm_done")
        o_hi, o_lo = sem("o_hi"), sem("o_lo")
        fc_done = sem("fc_done")
        y_done = sem("y_done")
        var_done, std_done, rstd_done = sem("var_done"), sem("std_done"), sem("rstd_done")
        ln_step, ln_done = sem("ln_step"), sem("ln_done")

        pool_passed, sp_passed = sem("pool_passed"), sem("sp_passed")

        ADDS = 2 * (KT - 1)

        block = stack.enter_context(nc.Block())

        @block.sync
        def _(eng):
            def load_weights(first_column):
                for i, src in enumerate((W_qs, W_ks, W_vs)):
                    eng.dma_start(w_raw[:, i, :, :], src.rearrange("(c p) n -> p c n", p=P)
                                  [:, :, bass.ds(first_column, P)]).then_inc(w_in, 16)

            def load_wo(first_row):
                eng.dma_start(wo_raw[:, :], fc_w[bass.ds(first_row, P), :]).then_inc(wo_in, 16)

            load_weights(0)
            ctx_tiles = ctx_in.rearrange("b (t p) d -> p (b t) d", p=P)
            for t in range(0, B * QT, QT):
                eng.dma_start(y[:, t:t + QT, :], x.rearrange("b (t p) d -> p (b t) d", p=P)[:, t:t + QT, :]) \
                    .then_inc(x_in[t // QT], 16)
            for t in range(0, B * KT, KT // 2):
                eng.dma_start(ctx_raw[:, t:t + KT // 2, :], ctx_tiles[:, t:t + KT // 2, :]).then_inc(ctx_loaded[t // (KT // 2)], 16)
            load_wo(0)
            eng.dma_start(fcb_row, fc_b.rearrange("(a n) -> a n", a=1).broadcast_to([P, D])).then_inc(fcb_in, 16)

            def phase(ph):
                if not (ph.attend and ph.load_pair):
                    return
                at = (ph.pair + 1) * P
                if ph.batch == 0:
                    eng.wait_ge(wqk_split, ph.pair + 1)
                    eng.wait_ge(wv_split, ph.pair + 1)
                    eng.sem_inc(sp_passed, 1)
                    load_weights(at)
                else:
                    eng.wait_ge(wo_split, ph.pair + 1)
                    eng.sem_inc(sp_passed, 1)
                    load_wo(at)

            run_phases(eng, phase)
            eng.wait_ge(wqk_split, PAIRS)
            eng.wait_ge(wv_split, PAIRS)
            eng.dma_start(g_row, ln_g.rearrange("(a n) -> a n", a=1).broadcast_to([P, D])).then_inc(gb_in, 16)
            eng.dma_start(b_row, ln_b.rearrange("(a n) -> a n", a=1).broadcast_to([P, D])).then_inc(gb_in, 16)
            out_tiles = out.rearrange("b (t p) d -> p (b t) d", p=P)
            for t in range(0, B * QT, 2):
                eng.wait_ge(ln_done, t + 2)
                eng.dma_start(out_tiles[:, t:t + 2, :], y[:, t:t + 2, :]).then_inc(stored, 16)
            eng.wait_ge(stored, 16 * (B * QT // 2))

        @block.gpsimd
        def _(eng):
            eng.memset(ident[:, :], 0.0).then_inc(consts_zero, 1)
            eng.wait_ge(consts_zero, 1)
            eng.affine_select(out=ident[:, :], in_=ident[:, :], compare_op=ALU.not_equal, fill=1.0, base=0,
                              pattern=[[-1, P]], channel_multiplier=1).then_inc(consts, 1)
            eng.memset(ones[:, :], 1.0).then_inc(consts, 1)
            eng.memset(eps[:, :], EPS).then_inc(consts, 1)

            def split_weights(pair):
                eng.wait_ge(w_in, 48 * (pair + 1))
                eng.sem_inc(pool_passed, 1)
                eng.tensor_copy(w[0][:, 0:2, :, :], w_raw[:, 0:2, :, :]).then_inc(wqk_hi, 1)
                eng.wait_ge(wqk_hi, pair + 1)
                eng.tensor_tensor(w[1][:, 0:2, :, :], w_raw[:, 0:2, :, :], w[0][:, 0:2, :, :].bitcast(F32),
                                  ALU.subtract).then_inc(wqk_split, 1)

            def split_wv(pair):
                eng.tensor_copy(w[0][:, 2, :, :], w_raw[:, 2, :, :]).then_inc(wv_hi, 1)
                eng.wait_ge(wv_hi, pair + 1)
                eng.tensor_tensor(w[1][:, 2, :, :], w_raw[:, 2, :, :], w[0][:, 2, :, :].bitcast(F32),
                                  ALU.subtract).then_inc(wv_split, 1)

            split_weights(0)
            split_wv(0)
            eng.wait_ge(fcb_in, 16)
            eng.wait_ge(turned, GROUPS // 3)
            for t in range(B * QT):
                eng.tensor_tensor(y[:, t, :], y[:, t, :], fcb_row, ALU.add).then_inc(y_init, 1)

            def phase(ph):
                n = ph.n
                if not ph.attend:
                    return
                if ph.batch == 1:
                    eng.wait_ge(wo_in, 16 * (ph.pair + 1))
                    if ph.after_two:
                        eng.wait_ge(fc_done, 4 * ph.pair)
                    eng.sem_inc(pool_passed, 1)
                    eng.tensor_copy(wo[0][:, :], wo_raw[:, :]).then_inc(wo_hi, 1)
                    eng.wait_ge(wo_hi, ph.pair + 1)
                    eng.tensor_tensor(wo[1][:, :], wo_raw[:, :], wo[0][:, :].bitcast(F32),
                                      ALU.subtract).then_inc(wo_split, 1)
                for head in range(2):
                    for kt in range(1, KT):
                        eng.wait_ge(exp_done, n * CHUNKS + head * KT + kt + 1)
                        if head == 0 and kt == 1 and ph.after_two:
                            eng.wait_ge(denom_done, n - 1)
                        if kt > 1:
                            eng.wait_ge(ksum_done, n * ADDS + head * (KT - 1) + kt - 1)
                        left = probs[ph.batch][:, head, 0, :] if kt == 1 else ksum[ph.batch][:, head, :]
                        eng.tensor_tensor(ksum[ph.batch][:, head, :], left, probs[ph.batch][:, head, kt, :],
                                          ALU.add).then_inc(ksum_done, 1)
                        if ph.batch == 0 and ph.load_pair and head == 0 and kt == 4:
                            eng.wait_ge(qk_done, 3 * (n + 2))
                            split_weights(ph.pair + 1)
                        if ph.batch == 0 and ph.load_pair and head == 1 and kt == 1:
                            eng.wait_ge(vT_done, 2 * (n + 2))
                            eng.sem_inc(pool_passed, 1)
                            split_wv(ph.pair + 1)

            run_phases(eng, phase)

        @block.tensor
        def _(eng):
            eng.wait_ge(consts, 1)
            for g in range(GROUPS):
                is_x = g < GROUPS // 3
                k = g if is_x else g - GROUPS // 3
                tile0, c = 4 * (k // CC), k % CC
                src = y if is_x else ctx_raw
                if c == 0:
                    eng.wait_ge((x_in if is_x else ctx_loaded)[k // CC], 16)
                if g >= 4:
                    eng.wait_ge(turned_lo, g - 3)
                for i in range(4):
                    last = nc.tensor.transpose(turn[g % 4][:, i * P:(i + 1) * P],
                                               src[:, tile0 + i, c * P:(c + 1) * P], ident[:, :])
                last.then_inc(turned, 1)

            def project(out_ap, which, acts, columns):
                for i, (a, b) in enumerate(PRODUCTS):
                    for c in range(CC):
                        last = nc.tensor.matmul(out_ap, w[a][:, which, c, :], acts[b][:, c, columns],
                                                start=(i == 0 and c == 0),
                                                stop=(i == len(PRODUCTS) - 1 and c == CC - 1))
                return last

            def phase(ph):
                n, me, other = ph.n, ph.batch, ph.other
                nxt = n + 1

                def project_q():
                    if not ph.prepare:
                        return
                    eng.wait_ge(wqk_split, ph.weights_split)
                    if ph.first:
                        eng.wait_ge(turned_lo, GROUPS)
                    elif ph.after_two:
                        eng.wait_ge(y_done, 2 * (n - 1))
                    if not ph.first:
                        eng.wait_ge(v_kept, 2 * nxt)
                    project(aux[0][:, :], 0, xT, slice(other * LQ, (other + 1) * LQ)).then_inc(qk_done, 1)

                def project_k(half):
                    if not ph.prepare:
                        return
                    if half == 1:
                        eng.wait_ge(qk_lo, 6 * nxt + 2)
                    at = other * LK + half * 512
                    project(aux[1 - half][:, :], 1, cT, slice(at, at + 512)).then_inc(qk_done, 1)

                def project_v(half):
                    if not ph.prepare:
                        return
                    if half == 0:
                        eng.wait_ge(wv_split, ph.weights_split)
                    eng.wait_ge(qk_lo, 6 * nxt + 4 + 2 * half)
                    at = other * LK + half * 512
                    project(aux[1 - half][:, :], 2, cT, slice(at, at + 512)).then_inc(vT_done, 1)

                def turn_v(half):
                    if not ph.prepare:
                        return
                    eng.wait_ge(vT_kept, 2 * nxt + half + 1)
                    for i in range(4):
                        last = nc.tensor.transpose(aux[1 - half][:, i * P:(i + 1) * P],
                                                   vT[:, half * 512 + i * P:half * 512 + (i + 1) * P], ident[:, :])
                    last.then_inc(vback_done, 1)

                def sweep_unit(u):
                    if not ph.prepare:
                        return
                    head, qt = divmod(u, QT)
                    if u == 0:
                        eng.wait_ge(qk_lo, 6 * nxt + 6)
                    if not (ph.first and u == 0):
                        eng.wait_ge(max_done, UNITS * nxt + u)
                    for half in range(KH):
                        last = nc.tensor.matmul(sweep[:, half * 512:(half + 1) * 512],
                                                qa[other][:, head, qt * P:(qt + 1) * P],
                                                ka[other][:, head, half * 512:(half + 1) * 512],
                                                start=True, stop=True)
                    last.then_inc(sweep_done, 1)

                def max_row(head):
                    if (head == 0 and not ph.prepare) or (head == 1 and not ph.attend):
                        return
                    if head == 0:
                        eng.wait_ge(max_done, UNITS * nxt + QT)
                        if ph.attend:
                            eng.wait_ge(row_kept, 2 * n + 2)
                    else:
                        eng.wait_ge(max_done, UNITS * n + 2 * QT)
                        if ph.finish:
                            eng.wait_ge(recip_done, n)
                        else:
                            eng.wait_ge(row_kept, 2 * n + 1)
                    for qt in range(QT):
                        column = negmax[:, head * QT + qt:head * QT + qt + 1]
                        last = nc.tensor.transpose(row[0:DH + 1, qt * P:(qt + 1) * P],
                                                   column.broadcast_to([P, DH + 1]),
                                                   ident[:, :])
                    last.then_inc(row_done, 1)

                def scores(c):
                    if not ph.attend:
                        return
                    head, kt = divmod(c, KT)
                    if kt == 0:
                        eng.wait_ge(row_kept, 2 * n + head + 1)
                    if ph.finish or c >= 2:
                        eng.wait_ge(exp_done, CHUNKS * n + c - 1)
                    keys = slice(kt * P, (kt + 1) * P)
                    nc.tensor.matmul(st[c % 2][:, :], ka[me][:, head, keys], qa[me][:, head, :],
                                     start=True, stop=False)
                    nc.tensor.matmul(st[c % 2][:, :], kb[me][0:DH + 1, head, keys], qb[me][0:DH + 1, head, :],
                                     start=False, stop=True).then_inc(st_done, 1)

                def times_v(kt):
                    if not ph.finish:
                        return
                    if kt == 0:
                        eng.wait_ge(exp_done, CHUNKS * n)
                        eng.wait_ge(v_kept, 2 * n)
                        if ph.after_two:
                            eng.wait_ge(norm_done, n - 1)
                    for head in range(2):
                        half = slice(head * DH, (head + 1) * DH)
                        last = nc.tensor.matmul(heads[half, :], v[other][:, kt, half], probs[other][:, head, kt, :],
                                                start=(kt == 0), stop=(kt == KT - 1))
                    if kt == KT - 1:
                        last.then_inc(heads_done, 1)

                def denominators():
                    if not ph.finish:
                        return
                    eng.wait_ge(ksum_done, ADDS * n)
                    if ph.attend:
                        eng.wait_ge(row_kept, 2 * n + 1)
                    else:
                        eng.wait_ge(recip_done, n - 1)
                    for head in range(2):
                        last = nc.tensor.matmul(row[head * DH:(head + 1) * DH, :], ones[:, :],
                                                ksum[other][:, head, :], start=True, stop=True)
                    last.then_inc(denom_done, 1)

                def project_out(half):
                    if not ph.finish:
                        return
                    if half == 0:
                        eng.wait_ge(o_lo, n)
                        eng.wait_ge(wo_split, ph.wo_split)
                    if ph.prepare:
                        eng.wait_ge(v_kept, 2 * nxt + half + 1)
                    else:
                        eng.wait_ge(y_done, 2 * (n - 1))
                    for t in range(2):
                        tokens = slice((2 * half + t) * P, (2 * half + t + 1) * P)
                        for i, (a, b) in enumerate(PRODUCTS):
                            last = nc.tensor.matmul(aux[1 - half][:, t * D:(t + 1) * D], o_part[a][:, tokens],
                                                    wo[b][:, :], start=(i == 0), stop=(i == len(PRODUCTS) - 1))
                    last.then_inc(fc_done, 1)

                if ph.first:
                    project_q()
                    project_k(0)
                    project_k(1)
                    project_v(0)
                    project_v(1)
                    eng.wait_ge(kb_ones, 2)
                    for u in range(UNITS):
                        sweep_unit(u)
                        if u == 2:
                            turn_v(0)
                        if u == 3:
                            turn_v(1)
                        if u == 5:
                            max_row(0)
                    return
                scores(0)
                scores(1)
                project_q()
                project_k(0)
                times_v(0)
                scores(2)
                scores(3)
                denominators()
                times_v(1)
                project_k(1)
                scores(4)
                times_v(2)
                scores(5)
                max_row(1)
                project_v(0)
                scores(6)
                sweep_unit(0)
                times_v(3)
                scores(7)
                project_v(1)
                sweep_unit(1)
                times_v(4)
                scores(8)
                sweep_unit(2)
                times_v(5)
                scores(9)
                sweep_unit(3)
                times_v(6)
                scores(10)
                sweep_unit(4)
                times_v(7)
                scores(11)
                sweep_unit(5)
                scores(12)
                turn_v(0)
                sweep_unit(6)
                scores(13)
                turn_v(1)
                max_row(0)
                scores(14)
                sweep_unit(7)
                scores(15)
                project_out(0)
                project_out(1)

            run_phases(eng, phase)

        @block.scalar
        def _(eng):
            for g in range(GROUPS):
                is_x = g < GROUPS // 3
                k = g if is_x else g - GROUPS // 3
                dst, at, c = (xT[0] if is_x else cT[0]), 512 * (k // CC), k % CC
                eng.wait_ge(turned, g + 1)
                nc.scalar.activation(dst[:, c, at:at + 512], turn[g % 4], ACT.Copy).then_inc(turned_hi, 1)

            def deviation(b):
                eng.wait_ge(var_done, b + 1)
                nc.scalar.activation(std[:, b * QT:(b + 1) * QT], meanvar[:, b * QT:(b + 1) * QT, 1], ACT.Sqrt,
                                     bias=eps[:, 0:1]).then_inc(std_done, 1)

            def phase(ph):
                n, me, other = ph.n, ph.batch, ph.other
                nxt = n + 1

                def hi_parts(group, head):
                    if not ph.prepare:
                        return
                    if head == 0:
                        eng.wait_ge(qk_done, 3 * nxt + group + 1)
                    src = aux[group % 2][head * DH:(head + 1) * DH, :]
                    if group == 0:
                        nc.scalar.activation(qa[other][0:DH, head, :], src, ACT.Copy, scale=SCALE)
                        nc.scalar.activation(qa[other][DH:P, head, :], src, ACT.Copy, scale=SCALE).then_inc(qk_hi, 1)
                    else:
                        at = (group - 1) * 512
                        nc.scalar.activation(ka[other][0:DH, head, at:at + 512], src, ACT.Copy)
                        nc.scalar.activation(kb[other][0:DH, head, at:at + 512], src, ACT.Copy).then_inc(qk_hi, 1)

                def keep_vT(half):
                    if not ph.prepare:
                        return
                    eng.wait_ge(vT_done, 2 * nxt + half + 1)
                    if half == 0 and not ph.first:
                        eng.wait_ge(vback_done, 2 * nxt)
                    nc.scalar.activation(vT[:, half * 512:(half + 1) * 512], aux[1 - half][:, :], ACT.Copy) \
                        .then_inc(vT_kept, 1)

                def keep_row(head):
                    if (head == 0 and not ph.prepare) or (head == 1 and not ph.attend):
                        return
                    s = other if head == 0 else me
                    eng.wait_ge(row_done, 2 * nxt + 1 if head == 0 else 2 * n + 2)
                    nc.scalar.activation(qb[s][DH:DH + 1, head, :], row[DH:DH + 1, :], ACT.Copy).then_inc(row_kept, 1)

                def exps(c):
                    if not ph.attend:
                        return
                    head, kt = divmod(c, KT)
                    if c == 0 and ph.after_two:
                        eng.wait_ge(heads_done, n - 1)
                        eng.wait_ge(ksum_done, ADDS * (n - 1))
                    if not ph.finish and c == 0:
                        eng.wait_ge(y_init, B * QT)
                    eng.wait_ge(st_done, CHUNKS * n + c + 1)
                    nc.scalar.activation(probs[me][:, head, kt, :], st[c % 2][:, :], ACT.Exp).then_inc(exp_done, 1)

                def heads_hi():
                    if not ph.finish:
                        return
                    eng.wait_ge(norm_done, n)
                    if ph.after_two:
                        eng.wait_ge(fc_done, 2 * (n - 1))
                    nc.scalar.activation(o_part[0][:, :], o_norm[:, :], ACT.Copy).then_inc(o_hi, 1)

                if ph.first:
                    for group in range(3):
                        hi_parts(group, 0)
                        hi_parts(group, 1)
                    keep_vT(0)
                    keep_vT(1)
                    keep_row(0)
                    return
                exps(0)
                exps(1)
                hi_parts(0, 0)
                hi_parts(0, 1)
                exps(2)
                hi_parts(1, 0)
                hi_parts(1, 1)
                exps(3)
                hi_parts(2, 0)
                hi_parts(2, 1)
                exps(4)
                exps(5)
                keep_row(1)
                keep_vT(0)
                exps(6)
                exps(7)
                keep_vT(1)
                for c in range(8, 13):
                    exps(c)
                heads_hi()
                exps(13)
                keep_row(0)
                exps(14)
                exps(15)
                if ph.last_attend:
                    deviation(0)

            run_phases(eng, phase)
            deviation(1)

        @block.vector
        def _(eng):
            for s in range(2):
                nc.vector.memset(kb[s][DH:DH + 1, :, :].bitcast(F32), 1.0).then_inc(kb_ones, 1)
            for g in range(GROUPS):
                is_x = g < GROUPS // 3
                k = g if is_x else g - GROUPS // 3
                i, at, c = (xT if is_x else cT), 512 * (k // CC), k % CC
                eng.wait_ge(turned_hi, g + 1)
                nc.vector.tensor_tensor(i[1][:, c, at:at + 512], turn[g % 4], i[0][:, c, at:at + 512].bitcast(F32),
                                        ALU.subtract).then_inc(turned_lo, 1)
            eng.wait_ge(y_init, B * QT)

            def layer_norm(b):
                eng.wait_ge(y_done, 2 * (PHASES - B + b + 1))
                for t in range(b * QT, (b + 1) * QT):
                    nc.vector.bn_stats(stats[:, t, :], y[:, t, :]).then_inc(ln_step, 1)
                for i, t in enumerate(range(b * QT, (b + 1) * QT)):
                    eng.wait_ge(ln_step, b * (4 * QT - 1) + i + 1)
                    last = nc.vector.bn_aggr(meanvar[:, t, :], stats[:, t, :])
                    if i < QT - 1:
                        last.then_inc(ln_step, 1)
                    else:
                        last.then_inc(var_done, 1)
                eng.wait_ge(std_done, b + 1)
                nc.vector.reciprocal(rstd[:, b * QT:(b + 1) * QT], std[:, b * QT:(b + 1) * QT]).then_inc(rstd_done, 1)
                eng.wait_ge(rstd_done, b + 1)
                eng.wait_ge(gb_in, 32)
                step = b * (4 * QT - 1) + 2 * QT - 1
                for t in range(b * QT, (b + 1) * QT):
                    nc.vector.tensor_scalar(y[:, t, :], y[:, t, :], meanvar[:, t, 0:1], rstd[:, t:t + 1],
                                            ALU.subtract, ALU.mult).then_inc(ln_step, 1)
                    step += 1
                    eng.wait_ge(ln_step, step)
                    nc.vector.tensor_tensor(y[:, t, :], y[:, t, :], g_row, ALU.mult).then_inc(ln_step, 1)
                    step += 1
                    eng.wait_ge(ln_step, step)
                    last = nc.vector.tensor_tensor(y[:, t, :], y[:, t, :], b_row, ALU.add)
                    last.then_inc(ln_done, 1)
                return step

            def phase(ph):
                n, me, other = ph.n, ph.batch, ph.other
                nxt = n + 1

                def lo_parts(group, head):
                    if not ph.prepare:
                        return
                    eng.wait_ge(qk_hi, 6 * nxt + 2 * group + head + 1)
                    src = aux[group % 2][head * DH:(head + 1) * DH, :]
                    if group == 0:
                        nc.vector.scalar_tensor_tensor(qb[other][0:DH, head, :], src, SCALE,
                                                       qa[other][0:DH, head, :].bitcast(F32),
                                                       ALU.mult, ALU.subtract).then_inc(qk_lo, 1)
                    else:
                        at = (group - 1) * 512
                        nc.vector.tensor_tensor(ka[other][DH:P, head, at:at + 512], src,
                                                ka[other][0:DH, head, at:at + 512].bitcast(F32),
                                                ALU.subtract).then_inc(qk_lo, 1)

                def unit_max(u):
                    if not ph.prepare:
                        return
                    eng.wait_ge(sweep_done, UNITS * nxt + u + 1)
                    nc.vector.tensor_reduce(negmax[:, u:u + 1], sweep[:, :], AX.X, ALU.max, negate=True) \
                        .then_inc(max_done, 1)

                def keep_v(half):
                    if not ph.prepare:
                        return
                    eng.wait_ge(vback_done, 2 * nxt + half + 1)
                    if ph.finish:
                        eng.wait_ge(heads_done, n)
                    nc.vector.tensor_copy(v[other][:, 4 * half:4 * half + 4, :],
                                          aux[1 - half][:, :].rearrange("p (t n) -> p t n", n=P)).then_inc(v_kept, 1)

                def reciprocals():
                    if not ph.finish:
                        return
                    eng.wait_ge(denom_done, n)
                    if ph.after_two:
                        eng.wait_ge(o_lo, n - 1)
                    nc.vector.reciprocal(o_norm[:, :], row[:, :]).then_inc(recip_done, 1)

                def normalise():
                    if not ph.finish:
                        return
                    eng.wait_ge(heads_done, n)
                    eng.wait_ge(recip_done, n)
                    nc.vector.tensor_tensor(o_norm[:, :], heads[:, :], o_norm[:, :], ALU.mult).then_inc(norm_done, 1)

                def heads_lo():
                    if not ph.finish:
                        return
                    eng.wait_ge(o_hi, n)
                    nc.vector.tensor_tensor(o_part[1][:, :], o_norm[:, :], o_part[0][:, :].bitcast(F32),
                                            ALU.subtract).then_inc(o_lo, 1)

                def add_y(half):
                    if not ph.finish:
                        return
                    eng.wait_ge(fc_done, 2 * (n - 1) + half + 1)
                    tiles = y[:, other * QT + 2 * half:other * QT + 2 * half + 2, :]
                    nc.vector.tensor_tensor(tiles, aux[1 - half][:, :].rearrange("p (t d) -> p t d", d=D), tiles,
                                            ALU.add).then_inc(y_done, 1)

                if ph.first:
                    for group in range(3):
                        lo_parts(group, 0)
                        lo_parts(group, 1)
                    for u in range(UNITS):
                        unit_max(u)
                        if u == 3:
                            keep_v(0)
                        if u == 4:
                            keep_v(1)
                    return
                for group in range(3):
                    if group == 2:
                        reciprocals()
                    lo_parts(group, 0)
                    lo_parts(group, 1)
                unit_max(0)
                for u in range(1, 5):
                    unit_max(u)
                normalise()
                unit_max(5)
                heads_lo()
                keep_v(0)
                unit_max(6)
                keep_v(1)
                unit_max(7)
                add_y(0)
                add_y(1)
                if ph.last_attend:
                    layer_norm(0)

            run_phases(eng, phase)
            layer_norm(1)


_INS = ['x', 'ctx_1024', 'L0_xattn_W_qs', 'L0_xattn_W_ks', 'L0_xattn_W_vs', 'L0_xattn_fc_w', 'L0_xattn_fc_b',
        'L0_xattn_ln_g', 'L0_xattn_ln_b']


def kernel(**inputs):
    import numpy as _np
    import concourse.bacc as _bacc
    from concourse import mybir as _mybir
    from concourse.bass_utils import run_bass_kernel_spmd as _run

    nc = _bacc.Bacc("TRN2", target_bir_lowering=False, num_devices=1)
    arrays, args = {}, []
    for name in _INS:
        a = _np.ascontiguousarray(inputs[name])
        arrays[f"in_{name}"] = a
        args.append(nc.dram_tensor(f"in_{name}", a.shape, _mybir.dt.from_np(a.dtype), kind="ExternalInput").ap())
    args.append(nc.dram_tensor("out_0", (B, LQ, D), _mybir.dt.float32, kind="ExternalOutput").ap())
    build(nc, *args)
    r = _run(nc, [arrays], core_ids=[0])
    return r.results[0]["out_0"]
```
